# Optimizing a Trainium2 kernel written in Bass

```python
import numpy as np
import jax
import jax.numpy as jnp

def _softmax(x, axis=-1):
    return jax.nn.softmax(x, axis=axis)

def _gelu(x):
    return jax.nn.gelu(x, approximate=True)

def _silu(x):
    return jax.nn.silu(x)

def _sigmoid(x):
    return jax.nn.sigmoid(x)

def _layernorm(x, axis=-1, eps=1e-05):
    m = jnp.mean(x, axis=axis, keepdims=True)
    v = jnp.var(x, axis=axis, keepdims=True)
    return (x - m) / jnp.sqrt(v + eps)

def _scatter_add(tgt, idx, src, axis=0):
    return tgt.at[idx].add(src)

def _segment_sum(src, seg, n):
    return jax.ops.segment_sum(src, seg, n)
kernel_name = 'mk_xattn_seq_d1_seqx_r8_5d478d'

def setup_inputs(seed: int=0):
    np.random.seed(seed)
    _w = jnp.asarray

    def _rec_inputs():
        import jax
        import jax.numpy as jnp
        _rk = jax.random.key(seed)
        x = -0.0002928 + 1 * jax.random.normal(jax.random.fold_in(_rk, 1), (1, 1024, 128), jnp.float32)
        _lenS = 1024 - jax.random.randint(jax.random.fold_in(_rk, 7), (1,), 0, max(1, 1024 // 4) + 1, jnp.int32)
        _lenS2 = 6404 - jax.random.randint(jax.random.fold_in(_rk, 8), (1,), 0, max(1, 6404 // 4) + 1, jnp.int32)
        _ctx_1024P = jax.random.normal(jax.random.fold_in(_rk, 11), (1, 16, 128), jnp.float32)
        _ctx_1024c = jax.random.dirichlet(jax.random.fold_in(_rk, 511), 0.3 * jnp.ones((16,), jnp.float32), (1, 6404))
        _ctx_1024t = jnp.einsum('bsk,bkd->bsd', _ctx_1024c, _ctx_1024P)
        _ctx_1024t = _ctx_1024t * jax.lax.rsqrt(jnp.mean(jnp.square(_ctx_1024t)) + 1e-12) * 0.953939
        ctx_1024 = -1.39393e-06 + 0.999914 * (_ctx_1024t + 0.3 * jax.random.normal(jax.random.fold_in(_rk, 611), (1, 6404, 128), jnp.float32))
        return (x, ctx_1024)
    x, ctx_1024 = _rec_inputs()

    def _L0_xattn_setup():
        import jax, jax.numpy as jnp
        import numpy as np
        N_HEADS, D_MODEL, D_K, D_V = (16, 128, 64, 64)
        B, S = (2, 256)
        key = jax.random.key(seed)
        k = jax.random.split(key, 7)
        s = 1.0 / np.sqrt(D_MODEL)
        return {'input_Q': jax.random.normal(k[0], (B, S, D_MODEL), jnp.float32), 'input_K': jax.random.normal(k[1], (B, S, D_MODEL), jnp.float32), 'input_V': jax.random.normal(k[2], (B, S, D_MODEL), jnp.float32), 'W_Q': jax.random.normal(k[3], (D_MODEL, N_HEADS * D_K), jnp.float32) * s, 'W_K': jax.random.normal(k[4], (D_MODEL, N_HEADS * D_K), jnp.float32) * s, 'W_V': jax.random.normal(k[5], (D_MODEL, N_HEADS * D_V), jnp.float32) * s, 'W_O': jax.random.normal(k[6], (N_HEADS * D_V, D_MODEL), jnp.float32) * s}
    _L0_xattn_all = _L0_xattn_setup()
    _L0_xattn_in = {k: v for k, v in _L0_xattn_all.items() if k in ('W_Q', 'W_K', 'W_V', 'W_O')}
    del _L0_xattn_all
    return {'x': x, 'ctx_1024': ctx_1024, 'L0_xattn_W_Q': _L0_xattn_in['W_Q'], 'L0_xattn_W_K': _L0_xattn_in['W_K'], 'L0_xattn_W_V': _L0_xattn_in['W_V'], 'L0_xattn_W_O': _L0_xattn_in['W_O']}

def reference(x, ctx_1024, L0_xattn_W_Q, L0_xattn_W_K, L0_xattn_W_V, L0_xattn_W_O):
    import jax
    import jax.numpy as jnp

    def _L0_xattn_ref(input_Q, input_K, input_V, W_Q, W_K, W_V, W_O):
        import jax, jax.numpy as jnp
        import numpy as np
        N_HEADS, D_MODEL, D_K, D_V = (16, 128, 64, 64)
        B, S = (2, 256)
        b = input_Q.shape[0]
        Q = (input_Q @ W_Q).reshape(b, -1, N_HEADS, D_K).transpose(0, 2, 1, 3)
        K = (input_K @ W_K).reshape(b, -1, N_HEADS, D_K).transpose(0, 2, 1, 3)
        V = (input_V @ W_V).reshape(b, -1, N_HEADS, D_V).transpose(0, 2, 1, 3)
        scores = jnp.einsum('bhqd,bhkd->bhqk', Q, K) / np.sqrt(D_K)
        attn = jax.nn.softmax(scores, axis=-1)
        context = jnp.einsum('bhqk,bhkd->bhqd', attn, V)
        context = context.transpose(0, 2, 1, 3).reshape(b, -1, N_HEADS * D_V)
        out = context @ W_O + input_Q
        mu = jnp.mean(out, axis=-1, keepdims=True)
        var = jnp.var(out, axis=-1, keepdims=True)
        return (out - mu) / jnp.sqrt(var + 1e-05)
    x = _L0_xattn_ref(x, ctx_1024, ctx_1024, L0_xattn_W_Q, L0_xattn_W_K, L0_xattn_W_V, L0_xattn_W_O)
    return x

_drawn_inputs = setup_inputs


def setup_inputs(seed=0):
    import zlib

    import numpy as np

    out = dict(_drawn_inputs(seed))
    spreads = {}
    factors = {}
    for name, (base, spread) in spreads.items():
        noise = np.random.default_rng([zlib.crc32(name.encode()), seed]).standard_normal(out[name].shape)
        drawn = base * np.exp(spread * noise) if base else spread * noise
        out[name] = jnp.asarray(drawn.astype(out[name].dtype))
    for name, factor in factors.items():
        out[name] = (out[name] * factor).astype(out[name].dtype)
    return out
```

```python
import concourse.bass as bass
from concourse import mybir
from contextlib import ExitStack

F32 = mybir.dt.float32
F32R = mybir.dt.float32r
I32 = mybir.dt.int32
ALU = mybir.AluOpType
ACT = mybir.ActivationFunctionType
AX = mybir.AxisListType


def cross_attention_kernel(nc: bass.Bass, xT: bass.AP, x: bass.AP, ctxT: bass.AP, w_q: bass.AP,
                           w_k: bass.AP, w_v: bass.AP, w_o: bass.AP, out: bass.AP):
    D, NQ = xT.shape
    NK = ctxT.shape[1]
    HD = w_q.shape[1]
    DH = 64
    PAIRS = HD // (2 * DH)
    SCALE = float(DH) ** -0.5
    P = 128
    QH = 512
    NQH = NQ // QH
    QT = NQ // P
    CHUNKS = -(-NK // P)
    LAST_KEYS = NK - (CHUNKS - 1) * P
    BLOCK = 4
    BK = BLOCK * P
    FULL_BLOCKS = NK // BK
    TAIL_KEYS = NK - FULL_BLOCKS * BK
    TAIL_COLS = (CHUNKS - FULL_BLOCKS * BLOCK) * P
    RING = 3
    TAIL_SLOT = RING
    RING_COLS = RING * BK + TAIL_COLS
    LOOP_STEPS = RING * BLOCK
    LOOPS = FULL_BLOCKS // RING - 1
    FIRST_STRAIGHT = 1 + LOOPS * LOOP_STEPS
    assert CHUNKS % RING == 0 and FULL_BLOCKS % RING == 0 and PAIRS % 2 == 0
    EPS = 1e-5
    SUM_MOST, SUM_LEAST = 1e20, 1e-20

    Q_STEPS = [FIRST_STRAIGHT, FIRST_STRAIGHT + 1, FIRST_STRAIGHT + 2, FIRST_STRAIGHT + 4]
    K_NEXT_STEP = 4 * FULL_BLOCKS

    def slot_of(b):
        return TAIL_SLOT if b == FULL_BLOCKS else b % RING

    def straight_uses(last):
        uses = []
        for c in range(CHUNKS):
            if c % BLOCK == 0 and c // BLOCK < FULL_BLOCKS:
                uses.append((c, ("k", c // BLOCK + 1)))
            if not last and c in Q_STEPS:
                uses.append((c, ("q", Q_STEPS.index(c))))
            if not last and c == K_NEXT_STEP:
                uses.append((c, ("k", 0)))
        return uses

    PRO_USES = 5
    PAIR_USES = len(straight_uses(False))
    NEXT_STEP_USE = {last: {c: (n, w) for n, (c, w) in enumerate(straight_uses(last))} for last in (False, True)}

    ctx = ExitStack()
    with ctx:
        def sb(name, shape, dt=F32):
            return ctx.enter_context(nc.sbuf_tensor(name, shape, dt))

        def pb(name, shape):
            return ctx.enter_context(nc.psum_tensor(name, shape, F32))

        def sem(name):
            return ctx.enter_context(nc.semaphore(name))

        xT_sb = sb("xT_sb", [P, NQ])
        x_sb = sb("x_sb", [P, QT, D])
        wo_sb = sb("wo_sb", [P, PAIRS, D])
        wq_dup = sb("wq_dup", [P, 2, 2, 2, DH])
        wk_sb = sb("wk_sb", [P, 2, 2 * DH])
        wv_sb = sb("wv_sb", [P, 2, 2 * DH])
        ctx_ring = sb("ctx_ring", [P, RING_COLS])
        k_parts = sb("k_parts", [P, 2, RING_COLS], F32R)
        q_parts = sb("q_parts", [P, 2, 2, 2, NQ], F32R)
        probs = sb("probs", [P, max(RING * 2 * NQ, CHUNKS * P)])
        v_ring = sb("v_ring", [P, RING, 2 * DH])
        sums = sb("sums", [P, 2, 2, NQ])
        o_raw = sb("o_raw", [P, NQ])
        inv_sum = sb("inv_sum", [P, NQ])
        limits = sb("limits", [P, 2, PAIRS * NQH])
        attn = sb("attn", [P, PAIRS, NQ])
        y = sb("y", [P, QT, D])
        stats = sb("stats", [P, QT, 6])
        mean_var = sb("mean_var", [P, QT, 2])
        inv_var = sb("inv_var", [P, QT])
        rstd = sb("rstd", [P, QT])
        ones = sb("ones", [P, DH])
        extremes = sb("extremes", [P, 2])
        in_range = sb("in_range", [P, 2])
        exact = sb("exact", [P, 1])
        use_general = sb("use_general", [1, 1], I32)

        g_row = probs[:, 0:CHUNKS * P]
        g_w = sb("g_w", [P, 3, 2 * DH])
        g_q = sb("g_q", [P, P])
        g_k = sb("g_k", [P, BK])
        g_v = sb("g_v", [P, 2 * DH])
        g_p = sb("g_p", [P, P])
        g_pT = sb("g_pT", [P, P])
        g_acc = sb("g_acc", [P, P])
        g_max = sb("g_max", [P, 1])
        g_bias = sb("g_bias", [P, 1])
        g_sum = sb("g_sum", [P, 1])
        g_inv = sb("g_inv", [P, 1])
        identity = sb("identity", [P, P])

        p_view = probs[:, 0:RING * 2 * NQ].rearrange("p (s h q) -> p s h q", s=RING, h=2)

        s_ps = pb("s_ps", [P, 2, NQ])
        o_ps = pb("o_ps", [P, NQ])
        kq_ps = pb("kq_ps", [P, QH])
        v_ps = pb("v_ps", [P, QH])
        den_ps = [kq_ps, v_ps]

        x_loaded = sem("x_loaded")
        xres_loaded = sem("xres_loaded")
        w_loaded = [sem(f"w_loaded{i}") for i in range(2)]
        ctx_loaded = [sem(f"ctx_loaded{i}") for i in range(RING + 1)]
        consts_ready = sem("consts_ready")
        kq_proj_done = sem("kq_proj_done")
        kq_high_ready = sem("kq_high_ready")
        kq_split = sem("kq_split")
        v_proj_done = sem("v_proj_done")
        v_ready = sem("v_ready")
        scores_ready = sem("scores_ready")
        probs_ready = sem("probs_ready")
        sums_done = sem("sums_done")
        pv_done = sem("pv_done")
        o_raw_ready = sem("o_raw_ready")
        den_done = sem("den_done")
        inv_ready = sem("inv_ready")
        limits_done = sem("limits_done")
        norm_done = sem("norm_done")
        y_done = sem("y_done")
        add_done = sem("add_done")
        ln_step = sem("ln_step")
        inv_var_ready = sem("inv_var_ready")
        rstd_ready = sem("rstd_ready")
        ln_done = sem("ln_done")
        stored = sem("stored")
        identity_ready = sem("identity_ready")
        range_step = sem("range_step")
        exact_ready = sem("exact_ready")
        exact_counted = sem("exact_counted")
        choice_ready = sem("choice_ready")
        g_w_loaded = sem("g_w_loaded")
        g_ctx_loaded = sem("g_ctx_loaded")
        g_q_done = sem("g_q_done")
        g_q_ready = sem("g_q_ready")
        g_k_done = sem("g_k_done")
        g_k_ready = sem("g_k_ready")
        g_s_done = sem("g_s_done")
        g_taken = sem("g_taken")
        g_row_step = sem("g_row_step")
        g_exp_done = sem("g_exp_done")
        g_p_ready = sem("g_p_ready")
        g_vp_done = sem("g_vp_done")
        g_vp_ready = sem("g_vp_ready")
        g_pv_done = sem("g_pv_done")
        g_attn_done = sem("g_attn_done")

        PV_CREDIT, SUM_CREDIT = RING, 2 * RING

        def use(pair, n):
            return PRO_USES + PAIR_USES * pair + n + 1

        def k_use(b, last):
            return [n for n, (_, w) in enumerate(straight_uses(last)) if w == ("k", b)][0]

        def run_pairs(eng, body):
            body(0, 0, True, False)
            with eng.Fori(0, PAIRS // 2 - 1) as i:
                for parity in (1, 0):
                    body(2 * i + (1 if parity else 2), parity, False, False)
            body(PAIRS - 1, 1, False, True)

        def run_steps(eng, step):
            step(0, 0, False)
            with eng.Fori(0, LOOPS) as j:
                for k in range(1, 1 + LOOP_STEPS):
                    step(LOOP_STEPS * j + k, k, True)
            for c in range(FIRST_STRAIGHT, CHUNKS):
                step(c, c, False)

        def cols_of(k, looped):
            b = k // BLOCK
            s = b % RING if looped else slot_of(b)
            return s * BK + (k % BLOCK) * P

        G_CHUNKS_TAIL = CHUNKS - FULL_BLOCKS * BLOCK
        G_BLOCKS = FULL_BLOCKS + 1
        G_TAKES = G_BLOCKS + CHUNKS

        def g_loops(eng, per_pair, per_tile, per_head):
            with eng.Fori(0, PAIRS) as pair:
                per_pair(pair)
                with eng.Fori(0, QT) as t:
                    per_tile(pair, t)
                    for head in range(2):
                        per_head(pair, t, head, 2 * QT * pair + 2 * t + head)

        def g_blocks(eng, body):
            with eng.Fori(0, FULL_BLOCKS) as b:
                body(b, 0)
            body(FULL_BLOCKS, TAIL_SLOT)

        def g_nothing(*_):
            pass

        def if_general(eng, program):
            eng.wait_ge(choice_ready, 1)
            chosen = eng.value_load(use_general[0:1, 0:1], min_val=0, max_val=1)
            with eng.If(chosen > 0):
                program()

        block = ctx.enter_context(nc.Block())

        @block.sync
        def _(sp):
            def load_w(pair, parity):
                cols = bass.ds(pair * 2 * DH, 2 * DH)
                src_q = w_q[:, cols].rearrange("p (h n) -> p h n", h=2)
                for copy in range(2):
                    sp.dma_start(wq_dup[:, parity, :, copy, :], src_q).then_inc(w_loaded[parity], 16)
                sp.dma_start(wk_sb[:, parity, :], w_k[:, cols]).then_inc(w_loaded[parity], 16)
                sp.dma_start(wv_sb[:, parity, :], w_v[:, cols]).then_inc(w_loaded[parity], 16)

            def load_ctx(b, s):
                n = TAIL_KEYS if s == TAIL_SLOT else BK
                sp.dma_start(ctx_ring[:, s * BK:s * BK + n],
                             ctxT[:, bass.ds(b * BK, n)]).then_inc(ctx_loaded[s], 16)

            load_w(0, 0)
            sp.dma_start(xT_sb[:, :], xT).then_inc(x_loaded, 16)
            for b in range(RING):
                load_ctx(b, b)
            load_w(1, 1)
            load_ctx(FULL_BLOCKS, TAIL_SLOT)
            sp.dma_start(x_sb[:, :, :], x.rearrange("(t p) d -> p t d", p=P)).then_inc(xres_loaded, 16)
            sp.dma_start(wo_sb[:, :, :], w_o.rearrange("(t p) d -> p t d", p=P)).then_inc(xres_loaded, 16)

            def rest_of_pair(pair, loop_eng):
                with loop_eng.Fori(1, FULL_BLOCKS // RING) as j:
                    for s in range(RING):
                        sp.wait_ge(v_proj_done, CHUNKS * pair + BLOCK * RING * j + (BLOCK * (s - RING) + BLOCK))
                        load_ctx(RING * j + s, s)

            rest_of_pair(0, sp)
            with sp.Fori(0, PAIRS // 2 - 1) as i:
                for parity in (1, 0):
                    pair = 2 * i + (1 if parity else 2)
                    for b in range(RING):
                        sp.wait_ge(v_proj_done, CHUNKS * pair - CHUNKS + BLOCK * (b + FULL_BLOCKS - RING + 1))
                        load_ctx(b, b)
                    sp.wait_ge(v_proj_done, CHUNKS * pair)
                    load_w(pair + 1, 1 - parity)
                    load_ctx(FULL_BLOCKS, TAIL_SLOT)
                    rest_of_pair(pair, sp)
            for b in range(RING):
                sp.wait_ge(v_proj_done, CHUNKS * (PAIRS - 2) + BLOCK * (b + FULL_BLOCKS - RING + 1))
                load_ctx(b, b)
            sp.wait_ge(v_proj_done, CHUNKS * (PAIRS - 1))
            load_ctx(FULL_BLOCKS, TAIL_SLOT)
            rest_of_pair(PAIRS - 1, sp)

            def general():
                def load_weights(pair):
                    sp.wait_ge(g_taken, G_TAKES * 2 * QT * pair + 1)
                    for n, w in enumerate((w_q, w_k, w_v)):
                        sp.dma_start(g_w[:, n, :], w[:, bass.ds(pair * 2 * DH, 2 * DH)]).then_inc(g_w_loaded, 16)

                def load_blocks(pair, t, head, n):
                    for taken, step in ((0, 1), (G_BLOCKS, BLOCK)):
                        with sp.Fori(0, FULL_BLOCKS) as b:
                            sp.wait_ge(g_taken, G_TAKES * n + b * step + taken + 1)
                            sp.dma_start(ctx_ring[:, 0:BK], ctxT[:, bass.ds(b * BK, BK)]).then_inc(g_ctx_loaded, 16)

                g_loops(sp, load_weights, g_nothing, load_blocks)

            if_general(sp, general)

            out_t = out.rearrange("(t p) d -> p t d", p=P)
            for h in range(2):
                sp.wait_ge(ln_done, (h + 1) * QT // 2)
                ts = slice(h * QT // 2, (h + 1) * QT // 2)
                sp.dma_start(out_t[:, ts, :], y[:, ts, :]).then_inc(stored, 16)
            sp.wait_ge(stored, 32)

        @block.gpsimd
        def _(pool):
            nc.gpsimd.memset(ctx_ring[:, RING * BK + TAIL_KEYS:RING_COLS], 0.0).then_inc(consts_ready, 1)
            nc.gpsimd.memset(ones[:, :], 1.0).then_inc(consts_ready, 1)
            nc.gpsimd.memset(identity[:, :], 0.0).then_inc(identity_ready, 1)
            pool.wait_ge(identity_ready, 1)
            nc.gpsimd.affine_select(out=identity[:, :], in_=identity[:, :], compare_op=ALU.not_equal, fill=1.0,
                                    base=0, pattern=[[-1, P]], channel_multiplier=1).then_inc(identity_ready, 1)

            def pair_end(pair, parity, first, last):
                for h in range(NQH):
                    q = slice(h * QH, (h + 1) * QH)
                    pool.wait_ge(inv_ready, NQH * pair + h + 1)
                    pool.wait_ge(o_raw_ready, NQH * pair + h + 1)
                    nc.gpsimd.tensor_tensor(out=attn[:, bass.ds(pair, 1), q].rearrange("p a q -> p (a q)"),
                                            in0=o_raw[:, q], in1=inv_sum[:, q], op=ALU.mult).then_inc(norm_done, 1)

            run_pairs(pool, pair_end)

        @block.tensor
        def _(pe):
            pe.sem_inc(pv_done, PV_CREDIT)

            def project_k(b_slot, parity, uses_before, first_use=False):
                n = TAIL_COLS if b_slot == TAIL_SLOT else BK
                pe.wait_ge(kq_split, uses_before)
                nc.tensor.matmul(kq_ps[:, 0:n], wk_sb[:, parity, :], ctx_ring[:, b_slot * BK:b_slot * BK + n],
                                 start=True, stop=True).then_inc(kq_proj_done, 1)

            def project_q(n, parity, uses_before):
                head, h = n // NQH, n % NQH
                if uses_before is not None:
                    pe.wait_ge(kq_split, uses_before)
                nc.tensor.matmul(kq_ps[:, :], wq_dup[:, parity, head, :, :].rearrange("p c n -> p (c n)"),
                                 xT_sb[:, h * QH:(h + 1) * QH], start=True, stop=True).then_inc(kq_proj_done, 1)

            def project_v(cols, parity, before):
                if before is not None:
                    pe.wait_ge(v_ready, before)
                nc.tensor.matmul(v_ps[:, 0:2 * DH], ctx_ring[:, cols:cols + P], wv_sb[:, parity, :],
                                 start=True, stop=True).then_inc(v_proj_done, 1)

            def scores(cols, parity, exps_before):
                for head in range(2):
                    if exps_before is not None:
                        pe.wait_ge(probs_ready, exps_before + head + 1)
                    for h in range(NQH):
                        q = slice(h * QH, (h + 1) * QH)
                        for part in range(2):
                            last = nc.tensor.matmul(s_ps[:, head, q], k_parts[:, head, cols:cols + P],
                                                    q_parts[:, parity, head, part, q],
                                                    start=(part == 0), stop=(part == 1))
                    last.then_inc(scores_ready, 1)

            def pv(p_slot, start, stop):
                for h in range(NQH):
                    q = slice(h * QH, (h + 1) * QH)
                    for head in range(2):
                        rows = slice(head * DH, (head + 1) * DH)
                        last = nc.tensor.matmul(o_ps[rows, q], v_ring[:, p_slot, rows], p_view[:, p_slot, head, q],
                                                start=start, stop=stop)
                last.then_inc(pv_done, 1)

            pe.wait_ge(w_loaded[0], 64)
            pe.wait_ge(x_loaded, 16)
            for n in range(4):
                project_q(n, 0, n if n else None)
            pe.wait_ge(ctx_loaded[0], 16)
            project_k(0, 0, 4)
            project_v(0, 0, None)
            pe.wait_ge(kq_split, PRO_USES)
            scores(0, 0, None)

            def pair_body(pair, parity, first, last):
                step_uses = NEXT_STEP_USE[last]
                g0 = CHUNKS * pair
                if not first:
                    pe.wait_ge(inv_ready, NQH * pair)

                def step(c, k, looped):
                    following = k + 1
                    at_end = not looped and following == CHUNKS
                    g = g0 + c
                    if at_end:
                        if not last:
                            pe.wait_ge(kq_split, use(pair, PAIR_USES - 1))
                            scores(0, 1 - parity, 2 * g)
                    else:
                        if following % BLOCK == 0:
                            if looped:
                                pe.wait_ge(kq_split, use(pair, 0) + (c - k) // BLOCK + (k + 1) // BLOCK - 1)
                            else:
                                pe.wait_ge(kq_split, use(pair, k_use(following // BLOCK, last)))
                        scores(cols_of(following, looped), parity, 2 * g)
                    if looped and k % BLOCK == 0:
                        s = (k // BLOCK + 1) % RING
                        loops_before = (c - k) // LOOP_STEPS
                        pe.wait_ge(ctx_loaded[s], (loops_before + (k // BLOCK + 1) // RING + 1
                                                   + pair * (FULL_BLOCKS // RING)) * 16)
                        project_k(s, parity, use(pair, 0) + (c - k) // BLOCK + k // BLOCK - 1)
                    if not looped and c in step_uses:
                        n, (what, b) = step_uses[c]
                        if what == "q":
                            if b == 0:
                                pe.wait_ge(w_loaded[1 - parity], w_need(pair, parity, first))
                            project_q(b, 1 - parity, use(pair, n) - 1)
                        elif b == 0:
                            pe.wait_ge(ctx_loaded[0], (pair + 1) * (16 * (FULL_BLOCKS // RING)) + 16)
                            project_k(0, 1 - parity, use(pair, n) - 1)
                        else:
                            s = slot_of(b)
                            if s == TAIL_SLOT:
                                if first:
                                    pe.wait_ge(consts_ready, 2)
                                pe.wait_ge(ctx_loaded[s], pair * 16 + 16)
                            else:
                                pe.wait_ge(ctx_loaded[s], pair * (16 * (FULL_BLOCKS // RING)) + 16 * (b // RING + 1))
                            project_k(s, parity, use(pair, n) - 1)
                    if at_end:
                        if not last:
                            project_v(0, 1 - parity, g + 1)
                    else:
                        project_v(cols_of(following, looped), parity, g + 1)
                    if not looped and k == 0 and not first:
                        pe.wait_ge(o_raw_ready, NQH * pair)
                    pe.wait_ge(v_ready, g + 1)
                    if at_end and last:
                        pe.wait_ge(probs_ready, 2 * g + 2)
                    pv(k % RING, not looped and k == 0, at_end)

                run_steps(pe, step)
                pe.wait_ge(sums_done, 2 * (g0 + CHUNKS) + SUM_CREDIT)
                if first:
                    pe.wait_ge(consts_ready, 2)
                for h in range(NQH):
                    if h == 0:
                        pe.wait_ge(kq_split, use(pair, len(straight_uses(last)) - 1))
                    else:
                        pe.wait_ge(v_ready, g0 + CHUNKS + (0 if last else 1))
                    for head in range(2):
                        rows = slice(head * DH, (head + 1) * DH)
                        last_mm = nc.tensor.matmul(den_ps[h][rows, :], ones[:, :],
                                                   sums[:, parity, head, h * QH:(h + 1) * QH], start=True, stop=True)
                    last_mm.then_inc(den_done, 1)

            def w_need(pair, parity, first):
                return 64 if first else 32 * pair + (32 + 64 if parity else 64)

            run_pairs(pe, pair_body)

            pe.wait_ge(exact_ready, 1)
            nc.tensor.matmul(s_ps[0:1, 0, 0:1], exact[:, :], ones[:, 0:1], start=True, stop=True).then_inc(exact_counted, 1)

            def general():
                pe.wait_ge(identity_ready, 2)

                def queries(pair, t):
                    pe.wait_ge(g_w_loaded, 48 * pair + 48)
                    pe.wait_ge(g_taken, G_TAKES * 2 * QT * pair + G_TAKES * 2 * t + 1)
                    nc.tensor.matmul(kq_ps[:, 0:P], g_w[:, 0, :], xT_sb[:, bass.ds(t * P, P)],
                                     start=True, stop=True).then_inc(g_q_done, 1)

                def head_of_tile(pair, t, head, n):
                    rows = slice(head * DH, (head + 1) * DH)

                    def block_scores(b, slot):
                        if slot != TAIL_SLOT:
                            pe.wait_ge(g_ctx_loaded, n * (32 * FULL_BLOCKS) + b * 16 + 16)
                        pe.wait_ge(g_q_ready, QT * pair + t + 1)
                        pe.wait_ge(g_taken, G_TAKES * n + b + 1)
                        cols = TAIL_COLS if slot == TAIL_SLOT else BK
                        nc.tensor.matmul(kq_ps[:, 0:cols], g_w[:, 1, :], ctx_ring[:, slot * BK:slot * BK + cols],
                                         start=True, stop=True).then_inc(g_k_done, 1)
                        pe.wait_ge(g_k_ready, G_BLOCKS * n + b + 1)
                        nc.tensor.matmul(s_ps[:, 0, 0:cols], g_q[rows, :], g_k[rows, 0:cols],
                                         start=True, stop=True).then_inc(g_s_done, 1)

                    g_blocks(pe, block_scores)

                    def block_product(b, slot):
                        if slot != TAIL_SLOT:
                            pe.wait_ge(g_ctx_loaded, n * (32 * FULL_BLOCKS) + b * 16 + (16 * FULL_BLOCKS + 16))
                        for m in range(G_CHUNKS_TAIL if slot == TAIL_SLOT else BLOCK):
                            k = CHUNKS * n + BLOCK * b + m
                            pe.wait_ge(g_p_ready, k + 1)
                            cols = slot * BK + m * P
                            nc.tensor.matmul(v_ps[:, 0:2 * DH], ctx_ring[:, cols:cols + P], g_w[:, 2, :],
                                             start=True, stop=True)
                            nc.tensor.transpose(kq_ps[:, 0:P], g_p[:, :], identity[:, :]).then_inc(g_vp_done, 1)
                            pe.wait_ge(g_vp_ready, k + 1)
                            nc.tensor.matmul(o_ps[rows, 0:P], g_v[:, rows], g_pT[:, :],
                                             start=True, stop=True).then_inc(g_pv_done, 1)

                    g_blocks(pe, block_product)

                g_loops(pe, g_nothing, queries, head_of_tile)
                pe.wait_ge(g_attn_done, 2 * QT * PAIRS)

            if_general(pe, general)

            y_ps = s_ps[:, :, :].rearrange("p h q -> p (h q)")
            pe.wait_ge(norm_done, NQH * PAIRS)
            pe.wait_ge(xres_loaded, 32)
            for t in range(QT):
                for pair in range(PAIRS):
                    last = nc.tensor.matmul(y_ps[:, (t % 4) * QH + (t // 4) * D:(t % 4) * QH + (t // 4 + 1) * D],
                                            attn[:, pair, t * P:(t + 1) * P],
                                            wo_sb[:, pair, :], start=(pair == 0), stop=(pair == PAIRS - 1))
                if t >= 4 or True:
                    last.then_inc(y_done, 1)

        @block.scalar
        def _(act):
            def high_k(slot):
                n = TAIL_COLS if slot == TAIL_SLOT else BK
                cols = slice(slot * BK, slot * BK + n)
                nc.scalar.activation(k_parts[0:DH, 0, cols], kq_ps[0:DH, 0:n], ACT.Copy)
                nc.scalar.activation(k_parts[DH:P, 1, cols], kq_ps[DH:P, 0:n], ACT.Copy).then_inc(kq_high_ready, 1)

            def high_q(n, parity):
                head, h = n // NQH, n % NQH
                nc.scalar.activation(q_parts[:, parity, head, 0, h * QH:(h + 1) * QH], kq_ps[:, :],
                                     ACT.Copy).then_inc(kq_high_ready, 1)

            def exps(g, p_slot):
                act.wait_ge(pv_done, g + (PV_CREDIT - RING + 1))
                act.wait_ge(sums_done, 2 * g + (SUM_CREDIT - 2 * RING + 2))
                for head in range(2):
                    act.wait_ge(scores_ready, 2 * g + head + 1)
                    nc.scalar.activation(p_view[:, p_slot, head, :], s_ps[:, head, :], ACT.Exp,
                                         scale=SCALE).then_inc(probs_ready, 1)

            for n in range(4):
                act.wait_ge(kq_proj_done, n + 1)
                high_q(n, 0)
            act.wait_ge(kq_proj_done, PRO_USES)
            high_k(0)
            exps(0, 0)

            def pair_body(pair, parity, first, last):
                g0 = CHUNKS * pair
                step_uses = NEXT_STEP_USE[last]

                def step(c, k, looped):
                    at_end = not looped and k + 1 == CHUNKS
                    if not (at_end and last):
                        exps(g0 + c + 1, (k + 1) % RING)
                    if looped and k % BLOCK == 0:
                        act.wait_ge(kq_proj_done, use(pair, 0) + (c - k) // BLOCK + k // BLOCK)
                        high_k((k // BLOCK + 1) % RING)
                    if not looped and c in step_uses:
                        n, (what, b) = step_uses[c]
                        act.wait_ge(kq_proj_done, use(pair, n))
                        if what == "q":
                            high_q(b, 1 - parity)
                        else:
                            high_k(slot_of(b))

                run_steps(act, step)
                act.wait_ge(pv_done, g0 + CHUNKS + PV_CREDIT)
                for h in range(NQH):
                    if not first:
                        act.wait_ge(norm_done, NQH * (pair - 1) + h + 1)
                    nc.scalar.activation(o_raw[:, h * QH:(h + 1) * QH], o_ps[:, h * QH:(h + 1) * QH],
                                         ACT.Copy).then_inc(o_raw_ready, 1)

            run_pairs(act, pair_body)
            def general():
                def head_of_tile(pair, t, head, n):
                    def copy_k(b, slot):
                        cols = TAIL_COLS if slot == TAIL_SLOT else BK
                        act.wait_ge(g_k_done, G_BLOCKS * n + b + 1)
                        nc.scalar.activation(g_k[:, 0:cols], kq_ps[:, 0:cols], ACT.Copy).then_inc(g_k_ready, 1)

                    g_blocks(act, copy_k)
                    act.wait_ge(g_row_step, 5 * n + 2)
                    nc.scalar.activation(g_row[:, 0:NK], g_row[:, 0:NK], ACT.Exp, bias=g_bias[:, 0:1], scale=SCALE,
                                         accum_out=g_sum[:, 0:1]).then_inc(g_exp_done, 1)

                    def copy_vp(b, slot):
                        for m in range(G_CHUNKS_TAIL if slot == TAIL_SLOT else BLOCK):
                            act.wait_ge(g_vp_done, CHUNKS * n + BLOCK * b + m + 1)
                            nc.scalar.activation(g_v[:, :], v_ps[:, 0:2 * DH], ACT.Copy)
                            nc.scalar.activation(g_pT[:, :], kq_ps[:, 0:P], ACT.Copy).then_inc(g_vp_ready, 1)

                    g_blocks(act, copy_vp)

                g_loops(act, g_nothing, g_nothing, head_of_tile)

            if_general(act, general)

            act.wait_ge(inv_var_ready, 1)
            nc.scalar.activation(rstd[:, :], inv_var[:, :], ACT.Sqrt).then_inc(rstd_ready, 1)

        @block.vector
        def _(dve):
            dve.sem_inc(sums_done, SUM_CREDIT)

            def low_k(slot):
                n = TAIL_COLS if slot == TAIL_SLOT else BK
                cols = slice(slot * BK, slot * BK + n)
                nc.vector.tensor_tensor(out=k_parts[DH:P, 0, cols], in0=kq_ps[0:DH, 0:n],
                                        in1=k_parts[0:DH, 0, cols].bitcast(F32), op=ALU.subtract)
                nc.vector.tensor_tensor(out=k_parts[0:DH, 1, cols], in0=kq_ps[DH:P, 0:n],
                                        in1=k_parts[DH:P, 1, cols].bitcast(F32), op=ALU.subtract).then_inc(kq_split, 1)

            def low_q(n, parity):
                head, h = n // NQH, n % NQH
                q = slice(h * QH, (h + 1) * QH)
                nc.vector.tensor_tensor(out=q_parts[:, parity, head, 1, q], in0=kq_ps[:, :],
                                        in1=q_parts[:, parity, head, 0, q].bitcast(F32),
                                        op=ALU.subtract).then_inc(kq_split, 1)

            def take_v(g, slot):
                dve.wait_ge(v_proj_done, g + 1)
                dve.wait_ge(pv_done, g + (PV_CREDIT - RING + 1))
                nc.vector.tensor_copy(v_ring[:, slot, :], v_ps[:, 0:2 * DH]).then_inc(v_ready, 1)

            def add_sums(g, p_slot, parity, new, rows):
                for head in range(2):
                    dve.wait_ge(probs_ready, 2 * g + head + 1)
                    if new:
                        nc.vector.tensor_copy(sums[:, parity, head, :], p_view[:, p_slot, head, :]).then_inc(sums_done, 1)
                    else:
                        dve.wait_ge(sums_done, 2 * g + head + (SUM_CREDIT - 1))
                        nc.vector.tensor_tensor(out=sums[0:rows, parity, head, :], in0=sums[0:rows, parity, head, :],
                                                in1=p_view[0:rows, p_slot, head, :], op=ALU.add).then_inc(sums_done, 1)

            for n in range(4):
                dve.wait_ge(kq_high_ready, n + 1)
                low_q(n, 0)
            dve.wait_ge(kq_high_ready, PRO_USES)
            low_k(0)
            take_v(0, 0)
            add_sums(0, 0, 0, True, P)

            def pair_body(pair, parity, first, last):
                g0 = CHUNKS * pair
                step_uses = NEXT_STEP_USE[last]

                def step(c, k, looped):
                    at_end = not looped and k + 1 == CHUNKS
                    g = g0 + c + 1
                    if not (at_end and last):
                        take_v(g, (k + 1) % RING)
                        if at_end:
                            add_sums(g, 0, 1 - parity, True, P)
                        else:
                            add_sums(g, (k + 1) % RING, parity, False,
                                     LAST_KEYS if not looped and k + 2 == CHUNKS else P)
                    if looped and k % BLOCK == 0:
                        dve.wait_ge(kq_high_ready, use(pair, 0) + (c - k) // BLOCK + k // BLOCK)
                        low_k((k // BLOCK + 1) % RING)
                    if not looped and c in step_uses:
                        n, (what, b) = step_uses[c]
                        dve.wait_ge(kq_high_ready, use(pair, n))
                        if what == "q":
                            low_q(b, 1 - parity)
                        else:
                            low_k(slot_of(b))

                run_steps(dve, step)
                for h in range(NQH):
                    dve.wait_ge(den_done, NQH * pair + h + 1)
                    if not first:
                        dve.wait_ge(norm_done, NQH * (pair - 1) + h + 1)
                    nc.vector.reciprocal(inv_sum[:, h * QH:(h + 1) * QH], den_ps[h][:, :]).then_inc(inv_ready, 1)
                for h in range(NQH):
                    dve.wait_ge(inv_ready, NQH * pair + h + 1)
                    for n, extreme in enumerate((ALU.max, ALU.min)):
                        nc.vector.tensor_reduce(out=limits[:, n, bass.ds(NQH * pair + h, 1)],
                                                in_=inv_sum[:, h * QH:(h + 1) * QH],
                                                axis=AX.X, op=extreme).then_inc(limits_done, 1)

            run_pairs(dve, pair_body)

            dve.wait_ge(limits_done, 2 * NQH * PAIRS)
            for n, extreme in enumerate((ALU.max, ALU.min)):
                nc.vector.tensor_reduce(out=extremes[:, n:n + 1], in_=limits[:, n, :], axis=AX.X,
                                        op=extreme).then_inc(range_step, 1)
            dve.wait_ge(range_step, 2)
            for n, (bound, within) in enumerate(((1 / SUM_LEAST, ALU.is_le), (1 / SUM_MOST, ALU.is_ge))):
                nc.vector.tensor_scalar(out=in_range[:, n:n + 1], in0=extremes[:, n:n + 1], scalar1=bound, scalar2=None,
                                        op0=within).then_inc(range_step, 1)
            dve.wait_ge(range_step, 4)
            nc.vector.tensor_tensor(out=exact[:, :], in0=in_range[:, 0:1], in1=in_range[:, 1:2],
                                    op=ALU.mult).then_inc(exact_ready, 1)
            dve.wait_ge(exact_counted, 1)
            nc.vector.tensor_scalar(out=use_general[:, :], in0=s_ps[0:1, 0, 0:1], scalar1=P - 0.5, scalar2=None,
                                    op0=ALU.is_lt).then_inc(choice_ready, 1)

            def general():
                dve.wait_ge(norm_done, NQH * PAIRS)
                dve.sem_inc(g_taken, 1)
                nc.vector.memset(g_row[:, NK:CHUNKS * P], 0.0)

                def queries(pair, t):
                    dve.wait_ge(g_q_done, QT * pair + t + 1)
                    nc.vector.tensor_copy(g_q[:, :], kq_ps[:, 0:P]).then_inc(g_q_ready, 1)

                def head_of_tile(pair, t, head, n):
                    rows = slice(head * DH, (head + 1) * DH)

                    def take_scores(b, slot):
                        cols = TAIL_KEYS if slot == TAIL_SLOT else BK
                        dve.wait_ge(g_s_done, G_BLOCKS * n + b + 1)
                        nc.vector.tensor_copy(g_row[:, bass.ds(b * BK, cols)], s_ps[:, 0, 0:cols]).then_inc(g_taken, 1)

                    g_blocks(dve, take_scores)
                    dve.wait_ge(g_taken, G_TAKES * n + (G_BLOCKS + 1))
                    nc.vector.tensor_reduce(out=g_max[:, :], in_=g_row[:, 0:NK], axis=AX.X,
                                            op=ALU.max).then_inc(g_row_step, 1)
                    dve.wait_ge(g_row_step, 5 * n + 1)
                    nc.vector.tensor_scalar(out=g_bias[:, :], in0=g_max[:, :], scalar1=-SCALE, scalar2=None,
                                            op0=ALU.mult).then_inc(g_row_step, 1)
                    dve.wait_ge(g_exp_done, n + 1)
                    nc.vector.reciprocal(g_inv[:, :], g_sum[:, :]).then_inc(g_row_step, 1)
                    dve.wait_ge(g_row_step, 5 * n + 3)
                    nc.vector.tensor_scalar(out=g_row[:, 0:NK], in0=g_row[:, 0:NK], scalar1=g_inv[:, 0:1], scalar2=None,
                                            op0=ALU.mult).then_inc(g_row_step, 1)
                    dve.wait_ge(g_row_step, 5 * n + 4)
                    nc.vector.memset(g_acc[rows, :], 0.0).then_inc(g_row_step, 1)

                    def take_products(b, slot):
                        for m in range(G_CHUNKS_TAIL if slot == TAIL_SLOT else BLOCK):
                            nc.vector.tensor_copy(g_p[:, :], g_row[:, bass.ds(b * BK + m * P, P)]).then_inc(g_p_ready, 1)
                            dve.wait_ge(g_row_step, 5 * n + 5)
                            dve.wait_ge(g_pv_done, CHUNKS * n + BLOCK * b + m + 1)
                            dve.wait_ge(g_taken, G_TAKES * n + BLOCK * b + (G_BLOCKS + m + 1))
                            nc.vector.tensor_tensor(out=g_acc[rows, :], in0=g_acc[rows, :], in1=o_ps[rows, 0:P],
                                                    op=ALU.add).then_inc(g_taken, 1)

                    g_blocks(dve, take_products)
                    dve.wait_ge(g_taken, G_TAKES * n + (G_TAKES + 1))
                    nc.vector.tensor_copy(attn[rows, bass.ds(pair, 1), bass.ds(t * P, P)].rearrange("p a q -> p (a q)"),
                                          g_acc[rows, :]).then_inc(g_attn_done, 1)

                g_loops(dve, g_nothing, queries, head_of_tile)

            if_general(dve, general)

            y_ps = s_ps[:, :, :].rearrange("p h q -> p (h q)")
            dve.wait_ge(xres_loaded, 32)
            for t in range(QT):
                dve.wait_ge(y_done, min(t + 5, QT))
                nc.vector.tensor_tensor(out=y[:, t, :], in0=y_ps[:, (t % 4) * QH + (t // 4) * D:(t % 4) * QH + (t // 4 + 1) * D],
                                        in1=x_sb[:, t, :], op=ALU.add).then_inc(ln_step, 1)
            for t in range(QT):
                dve.wait_ge(ln_step, t + 1)
                nc.vector.bn_stats(stats[:, t, :], y[:, t, :]).then_inc(ln_step, 1)
            for t in range(QT):
                dve.wait_ge(ln_step, QT + t + 1)
                nc.vector.bn_aggr(mean_var[:, t, :], stats[:, t, :]).then_inc(ln_step, 1)
            dve.wait_ge(ln_step, 3 * QT)
            nc.vector.tensor_scalar(out=inv_var[:, :], in0=mean_var[:, :, 1], scalar1=EPS, scalar2=None,
                                    op0=ALU.add).then_inc(ln_step, 1)
            dve.wait_ge(ln_step, 3 * QT + 1)
            nc.vector.reciprocal(inv_var[:, :], inv_var[:, :]).then_inc(inv_var_ready, 1)
            dve.wait_ge(rstd_ready, 1)
            for t in range(QT):
                nc.vector.tensor_scalar(out=y[:, t, :], in0=y[:, t, :], scalar1=mean_var[:, t, 0:1],
                                        scalar2=rstd[:, t:t + 1], op0=ALU.subtract,
                                        op1=ALU.mult).then_inc(ln_done, 1)


def kernel(**inputs):
    import numpy as np
    import concourse.bacc as bacc
    from concourse import mybir as mb
    from concourse.bass_utils import run_bass_kernel_spmd

    x = np.asarray(inputs["x"])[0]
    context = np.asarray(inputs["ctx_1024"])[0]
    arrays = {
        "in_xT": np.ascontiguousarray(x.T),
        "in_x": np.ascontiguousarray(x),
        "in_ctxT": np.ascontiguousarray(context.T),
        "in_wq": np.ascontiguousarray(inputs["L0_xattn_W_Q"]),
        "in_wk": np.ascontiguousarray(inputs["L0_xattn_W_K"]),
        "in_wv": np.ascontiguousarray(inputs["L0_xattn_W_V"]),
        "in_wo": np.ascontiguousarray(inputs["L0_xattn_W_O"]),
    }
    nc = bacc.Bacc("TRN2", target_bir_lowering=False, num_devices=1)
    args = [nc.dram_tensor(n, a.shape, mb.dt.from_np(a.dtype), kind="ExternalInput").ap() for n, a in arrays.items()]
    out = nc.dram_tensor("out_0", x.shape, mb.dt.from_np(x.dtype), kind="ExternalOutput").ap()
    cross_attention_kernel(nc, *args, out)
    r = run_bass_kernel_spmd(nc, [arrays], core_ids=[0])
    return r.results[0]["out_0"].reshape(1, *x.shape)
```

```python
import concourse.bass as bass
from concourse import mybir
from contextlib import ExitStack

F32 = mybir.dt.float32
F32R = mybir.dt.float32r
I32 = mybir.dt.int32
ALU = mybir.AluOpType
ACT = mybir.ActivationFunctionType
AX = mybir.AxisListType


def cross_attention_kernel(nc: bass.Bass, xT: bass.AP, x: bass.AP, ctxT: bass.AP, w_q: bass.AP,
                           w_k: bass.AP, w_v: bass.AP, w_o: bass.AP, out: bass.AP):
    D, NQ = xT.shape
    NK = ctxT.shape[1]
    HD = w_q.shape[1]
    DH = 64
    PAIRS = HD // (2 * DH)
    SCALE = float(DH) ** -0.5
    P = 128
    QH = 512
    NQH = NQ // QH
    QT = NQ // P
    CHUNKS = -(-NK // P)
    LAST_KEYS = NK - (CHUNKS - 1) * P
    BLOCK = 4
    BK = BLOCK * P
    FULL_BLOCKS = NK // BK
    TAIL_KEYS = NK - FULL_BLOCKS * BK
    TAIL_COLS = (CHUNKS - FULL_BLOCKS * BLOCK) * P
    RING = 3
    TAIL_SLOT = RING
    RING_COLS = RING * BK + TAIL_COLS
    LOOP_CHUNKS = RING * BLOCK
    LOOPS = FULL_BLOCKS // RING - 1
    FIRST_STRAIGHT = 1 + LOOPS * LOOP_CHUNKS
    V_GROUPS = (CHUNKS + 1) // 2
    assert CHUNKS % RING == 0 and FULL_BLOCKS % RING == 0 and PAIRS % 2 == 0
    assert CHUNKS % 2 == 1 and V_GROUPS % 2 == 0 and LOOP_CHUNKS % 4 == 0
    EPS = 1e-5
    WARM_UP = 2
    SUM_MOST, SUM_LEAST = 1e20, 1e-20

    def straight_uses(last):
        c = FIRST_STRAIGHT
        uses = {(0, "mid"): ("k", 1), (c + 2, "mid"): ("k", FULL_BLOCKS - 1), (c + 6, "mid"): ("k", FULL_BLOCKS)}
        if not last:
            uses.update({(c, "mid"): ("q", 0), (c, "end"): ("q", 1), (c + 4, "mid"): ("q", 2),
                         (c + 8, "mid"): ("q", 3), (c + 10, "mid"): ("k", 0)})
        return uses

    INV_PIECES = 4
    INV_STEPS = [FIRST_STRAIGHT + 2 + 2 * n for n in range(INV_PIECES)]
    LIMIT_STEPS = [INV_STEPS[-1] + 2, INV_STEPS[-1] + 4]

    def slot_of(b):
        return TAIL_SLOT if b == FULL_BLOCKS else b % RING

    LOOP_USES = LOOPS * RING

    def numbered(last):
        ordered = sorted(straight_uses(last), key=lambda at: (at[0], at[1] == "end"))
        return {at: (n + (LOOP_USES if n else 0), *straight_uses(last)[at]) for n, at in enumerate(ordered)}

    STRAIGHT_USES = {last: numbered(last) for last in (False, True)}
    PRO_USES = 5
    PAIR_USES = len(straight_uses(False)) + LOOP_USES

    ctx = ExitStack()
    with ctx:
        def sb(name, shape, dt=F32):
            return ctx.enter_context(nc.sbuf_tensor(name, shape, dt))

        def pb(name, shape):
            return ctx.enter_context(nc.psum_tensor(name, shape, F32))

        def sem(name):
            return ctx.enter_context(nc.semaphore(name))

        xT_sb = sb("xT_sb", [P, NQ])
        x_sb = sb("x_sb", [P, QT, D])
        wo_sb = sb("wo_sb", [P, PAIRS, D])
        wq_dup = sb("wq_dup", [P, 2, 2, 2, DH])
        wk_sb = sb("wk_sb", [P, 2, 2 * DH])
        wv_sb = sb("wv_sb", [P, 2, 2 * DH])
        ctx_ring = sb("ctx_ring", [P, RING_COLS])
        k_parts = sb("k_parts", [P, 2, RING_COLS], F32R)
        q_parts = sb("q_parts", [P, 2, 2, 2, NQ], F32R)
        probs = sb("probs", [P, max(RING * 2 * NQ, CHUNKS * P)])
        v_ring = sb("v_ring", [P, 2, 2, 2 * DH])
        sums = sb("sums", [P, 2, 2, NQ])
        o_raw = sb("o_raw", [P, NQ])
        inv_sum = sb("inv_sum", [P, NQ])
        limits = sb("limits", [P, 2, PAIRS])
        attn = sb("attn", [P, PAIRS, NQ])
        y = sb("y", [P, QT, D])
        stats = sb("stats", [P, QT, 6])
        mean_var = sb("mean_var", [P, QT, 2])
        inv_var = sb("inv_var", [P, QT])
        rstd = sb("rstd", [P, QT])
        ones = sb("ones", [P, DH])
        extremes = sb("extremes", [P, 2])
        in_range = sb("in_range", [P, 2])
        exact = sb("exact", [P, 1])
        use_general = sb("use_general", [1, 1], I32)

        g_row = probs[:, 0:CHUNKS * P]
        g_w = sb("g_w", [P, 3, 2 * DH])
        g_q = sb("g_q", [P, P])
        g_k = sb("g_k", [P, BK])
        g_v = sb("g_v", [P, 2 * DH])
        g_p = sb("g_p", [P, P])
        g_pT = sb("g_pT", [P, P])
        g_acc = sb("g_acc", [P, P])
        g_max = sb("g_max", [P, 1])
        g_bias = sb("g_bias", [P, 1])
        g_sum = sb("g_sum", [P, 1])
        g_inv = sb("g_inv", [P, 1])
        identity = sb("identity", [P, P])

        p_view = probs[:, 0:RING * 2 * NQ].rearrange("p (s h q) -> p s h q", s=RING, h=2)

        s_ps = pb("s_ps", [P, 2, NQ])
        o_ps = pb("o_ps", [P, NQ])
        kq_ps = pb("kq_ps", [P, QH])
        v_ps = pb("v_ps", [P, QH])
        den_ps = [kq_ps, v_ps]
        q0_ps = [o_ps[:, 0:QH], o_ps[:, QH:NQ], s_ps[:, 1, 0:QH], s_ps[:, 1, QH:NQ]]
        y_ps = [s_ps[:, 0, 0:D], s_ps[:, 0, QH:QH + D], s_ps[:, 1, 0:D], s_ps[:, 1, QH:QH + D],
                o_ps[:, 0:D], o_ps[:, QH:QH + D], kq_ps[:, 0:D], v_ps[:, 0:D]]

        x_loaded = sem("x_loaded")
        xres_loaded = sem("xres_loaded")
        w_loaded = [sem(f"w_loaded{i}") for i in range(2)]
        ctx_loaded = [sem(f"ctx_loaded{i}") for i in range(RING + 1)]
        wq0_loaded = sem("wq0_loaded")
        wv0_loaded = sem("wv0_loaded")
        zeros_ready = sem("zeros_ready")
        consts_ready = sem("consts_ready")
        kq_proj_done = sem("kq_proj_done")
        kq_high_ready = sem("kq_high_ready")
        kq_split = sem("kq_split")
        v_proj_done = sem("v_proj_done")
        v_ready = sem("v_ready")
        scores_ready = sem("scores_ready")
        probs_ready = sem("probs_ready")
        sums_done = sem("sums_done")
        pv_done = sem("pv_done")
        o_raw_ready = sem("o_raw_ready")
        den_done = sem("den_done")
        den_taken = sem("den_taken")
        inv_ready = sem("inv_ready")
        limits_done = sem("limits_done")
        norm_done = sem("norm_done")
        y_done = sem("y_done")
        y_taken = sem("y_taken")
        ln_step = sem("ln_step")
        table_loaded = sem("table_loaded")
        inv_var_ready = sem("inv_var_ready")
        rstd_ready = sem("rstd_ready")
        ln_done = sem("ln_done")
        stored = sem("stored")
        identity_ready = sem("identity_ready")
        range_step = sem("range_step")
        exact_ready = sem("exact_ready")
        exact_counted = sem("exact_counted")
        choice_ready = sem("choice_ready")
        g_w_loaded = sem("g_w_loaded")
        g_ctx_loaded = sem("g_ctx_loaded")
        g_q_done = sem("g_q_done")
        g_q_ready = sem("g_q_ready")
        g_k_done = sem("g_k_done")
        g_k_ready = sem("g_k_ready")
        g_s_done = sem("g_s_done")
        g_taken = sem("g_taken")
        g_row_step = sem("g_row_step")
        g_exp_done = sem("g_exp_done")
        g_p_ready = sem("g_p_ready")
        g_vp_done = sem("g_vp_done")
        g_vp_ready = sem("g_vp_ready")
        g_pv_done = sem("g_pv_done")
        g_attn_done = sem("g_attn_done")

        PV_CREDIT, SUM_CREDIT = RING, 2 * RING

        def use(pair, n):
            return PRO_USES + PAIR_USES * pair + n + 1

        def k_use(b, last):
            if 1 < b <= LOOP_USES + 1:
                return b - 1
            return [n for n, what, m in STRAIGHT_USES[last].values() if (what, m) == ("k", b)][0]

        def groups(pair, n):
            return V_GROUPS * pair + n + 2

        def v_place(k):
            return (1, 1) if k in (0, CHUNKS) else (k // 2 % 2, k % 2)

        def run_pairs(eng, body):
            body(0, 0, True, False)
            with eng.Fori(0, PAIRS // 2 - 1) as i:
                for parity in (1, 0):
                    body(2 * i + (1 if parity else 2), parity, False, False)
            body(PAIRS - 1, 1, False, True)

        def run_steps(eng, step):
            step(0, 0, False)
            with eng.Fori(0, LOOPS) as j:
                for k in range(1, 1 + LOOP_CHUNKS, 2):
                    step(LOOP_CHUNKS * j + k, k, True)
            for c in range(FIRST_STRAIGHT, CHUNKS, 2):
                step(c, c, False)

        def chunks_of(c, k):
            return [(c + 1, k + 1)] if k == 0 else [(c + 1, k + 1), (c + 2, k + 2)]

        def use_in(pair, c, k, looped, place, last):
            if looped:
                if place == "mid" and (k + 1) % BLOCK == 0:
                    n = (k + 1) // BLOCK
                    return use(pair, 0) + (c - k) // BLOCK + n, "k", None, (n + 1) % RING
            elif (c, place) in STRAIGHT_USES[last]:
                n, what, b = STRAIGHT_USES[last][c, place]
                return use(pair, n), what, b, slot_of(b)

        def cols_of(k, looped):
            b = k // BLOCK
            s = b % RING if looped else slot_of(b)
            return s * BK + (k % BLOCK) * P

        G_CHUNKS_TAIL = CHUNKS - FULL_BLOCKS * BLOCK
        G_BLOCKS = FULL_BLOCKS + 1
        G_TAKES = G_BLOCKS + CHUNKS

        def g_loops(eng, per_pair, per_tile, per_head):
            with eng.Fori(0, PAIRS) as pair:
                per_pair(pair)
                with eng.Fori(0, QT) as t:
                    per_tile(pair, t)
                    for head in range(2):
                        per_head(pair, t, head, 2 * QT * pair + 2 * t + head)

        def g_blocks(eng, body):
            with eng.Fori(0, FULL_BLOCKS) as b:
                body(b, 0)
            body(FULL_BLOCKS, TAIL_SLOT)

        def g_nothing(*_):
            pass

        def if_general(eng, program):
            eng.wait_ge(choice_ready, 1)
            chosen = eng.value_load(use_general[0:1, 0:1], min_val=0, max_val=1)
            with eng.If(chosen > 0):
                program()

        block = ctx.enter_context(nc.Block())

        @block.sync
        def _(sp):
            def load_w(pair, parity):
                cols = bass.ds(pair * 2 * DH, 2 * DH)
                src_q = w_q[:, cols].rearrange("p (h n) -> p h n", h=2)
                for copy in range(2):
                    sp.dma_start(wq_dup[:, parity, :, copy, :], src_q).then_inc(w_loaded[parity], 16)
                sp.dma_start(wk_sb[:, parity, :], w_k[:, cols]).then_inc(w_loaded[parity], 16)
                sp.dma_start(wv_sb[:, parity, :], w_v[:, cols]).then_inc(w_loaded[parity], 16)

            def load_ctx(b, s):
                n = TAIL_KEYS if s == TAIL_SLOT else BK
                sp.dma_start(ctx_ring[:, s * BK:s * BK + n],
                             ctxT[:, bass.ds(b * BK, n)]).then_inc(ctx_loaded[s], 16)

            sp.dma_start(wk_sb[:, 0, :], w_k[:, 0:2 * DH]).then_inc(w_loaded[0], 16)
            load_ctx(0, 0)
            sp.dma_start(wv_sb[:, 0, :], w_v[:, 0:2 * DH]).then_inc(wv0_loaded, 16)
            for b in range(1, RING):
                load_ctx(b, b)
            load_w(1, 1)
            load_ctx(FULL_BLOCKS, TAIL_SLOT)
            sp.dma_start(x_sb[:, :, :], x.rearrange("(t p) d -> p t d", p=P)).then_inc(xres_loaded, 16)
            sp.dma_start(wo_sb[:, :, :], w_o.rearrange("(t p) d -> p t d", p=P)).then_inc(xres_loaded, 16)

            def rest_of_pair(pair, loop_eng):
                with loop_eng.Fori(1, FULL_BLOCKS // RING) as j:
                    for s in range(RING):
                        sp.wait_ge(v_proj_done, groups(pair, LOOP_CHUNKS // 2 * j + (BLOCK // 2 * (s - RING + 1) - 1)))
                        load_ctx(RING * j + s, s)

            rest_of_pair(0, sp)
            with sp.Fori(0, PAIRS // 2 - 1) as i:
                for parity in (1, 0):
                    pair = 2 * i + (1 if parity else 2)
                    for b in range(RING):
                        sp.wait_ge(v_proj_done, groups(pair - 1, BLOCK // 2 * (b + FULL_BLOCKS - RING + 1) - 1))
                        load_ctx(b, b)
                    sp.wait_ge(v_proj_done, groups(pair - 1, V_GROUPS - 1))
                    load_w(pair + 1, 1 - parity)
                    load_ctx(FULL_BLOCKS, TAIL_SLOT)
                    rest_of_pair(pair, sp)
            for b in range(RING):
                sp.wait_ge(v_proj_done, groups(PAIRS - 2, BLOCK // 2 * (b + FULL_BLOCKS - RING + 1) - 1))
                load_ctx(b, b)
            sp.wait_ge(v_proj_done, groups(PAIRS - 2, V_GROUPS - 1))
            load_ctx(FULL_BLOCKS, TAIL_SLOT)
            rest_of_pair(PAIRS - 1, sp)

            def general():
                def load_weights(pair):
                    sp.wait_ge(g_taken, G_TAKES * 2 * QT * pair + 1)
                    for n, w in enumerate((w_q, w_k, w_v)):
                        sp.dma_start(g_w[:, n, :], w[:, bass.ds(pair * 2 * DH, 2 * DH)]).then_inc(g_w_loaded, 16)

                def load_blocks(pair, t, head, n):
                    for taken, step in ((0, 1), (G_BLOCKS, BLOCK)):
                        with sp.Fori(0, FULL_BLOCKS) as b:
                            sp.wait_ge(g_taken, G_TAKES * n + b * step + taken + 1)
                            sp.dma_start(ctx_ring[:, 0:BK], ctxT[:, bass.ds(b * BK, BK)]).then_inc(g_ctx_loaded, 16)

                g_loops(sp, load_weights, g_nothing, load_blocks)

            def store(turn):
                for n in range(QT // 2):
                    sp.wait_ge(ln_done, QT * turn + 2 * n + 2)
                    sp.dma_start(out_t[:, 2 * n:2 * n + 2, :], y[:, 2 * n:2 * n + 2, :]).then_inc(stored, 16)

            def general_and_store():
                general()
                store(1)
                sp.wait_ge(stored, 2 * 16 * (QT // 2))

            out_t = out.rearrange("(t p) d -> p t d", p=P)
            store(0)
            sp.wait_ge(stored, 16 * (QT // 2))
            if_general(sp, general_and_store)

        @block.gpsimd
        def _(pool):
            nc.gpsimd.memset(ctx_ring[:, RING * BK + TAIL_KEYS:RING_COLS], 0.0).then_inc(consts_ready, 1)
            nc.gpsimd.memset(ones[:, :], 1.0).then_inc(consts_ready, 1)
            nc.gpsimd.memset(identity[:, :], 0.0).then_inc(identity_ready, 1)
            pool.wait_ge(identity_ready, 1)
            nc.gpsimd.affine_select(out=identity[:, :], in_=identity[:, :], compare_op=ALU.not_equal, fill=1.0,
                                    base=0, pattern=[[-1, P]], channel_multiplier=1).then_inc(identity_ready, 1)

            def pair_end(pair, parity, first, last):
                for h in range(NQH):
                    q = slice(h * QH, (h + 1) * QH)
                    pool.wait_ge(inv_ready, INV_PIECES * pair + (h + 1) * INV_PIECES // NQH)
                    pool.wait_ge(o_raw_ready, NQH * pair + h + 1)
                    nc.gpsimd.tensor_tensor(out=attn[:, bass.ds(pair, 1), q].rearrange("p a q -> p (a q)"),
                                            in0=o_raw[:, q], in1=inv_sum[:, q], op=ALU.mult).then_inc(norm_done, 1)

            run_pairs(pool, pair_end)

        @block.tensor
        def _(pe):
            pe.sem_inc(pv_done, PV_CREDIT)

            def project_k(b_slot, parity, uses_before):
                n = TAIL_COLS if b_slot == TAIL_SLOT else BK
                if uses_before is not None:
                    pe.wait_ge(kq_split, uses_before)
                nc.tensor.matmul(kq_ps[:, 0:n], wk_sb[:, parity, :], ctx_ring[:, b_slot * BK:b_slot * BK + n],
                                 start=True, stop=True).then_inc(kq_proj_done, 1)

            def project_q(dst, n, parity):
                head, h = n // NQH, n % NQH
                nc.tensor.matmul(dst, wq_dup[:, parity, head, :, :].rearrange("p c n -> p (c n)"),
                                 xT_sb[:, h * QH:(h + 1) * QH], start=True, stop=True).then_inc(kq_proj_done, 1)

            def project_v(pos, cols, parity):
                return nc.tensor.matmul(v_ps[:, pos * P:(pos + 1) * P], ctx_ring[:, cols:cols + P],
                                        wv_sb[:, parity, :], start=True, stop=True)

            def scores(cols, parity, exps_before):
                for head in range(2):
                    if exps_before is not None:
                        pe.wait_ge(probs_ready, exps_before + head + 1)
                    for h in range(NQH):
                        q = slice(h * QH, (h + 1) * QH)
                        for part in range(2):
                            last = nc.tensor.matmul(s_ps[:, head, q], k_parts[:, head, cols:cols + P],
                                                    q_parts[:, parity, head, part, q],
                                                    start=(part == 0), stop=(part == 1))
                    last.then_inc(scores_ready, 1)

            def pv(p_slot, v_at, start, stop):
                for h in range(NQH):
                    q = slice(h * QH, (h + 1) * QH)
                    for head in range(2):
                        rows = slice(head * DH, (head + 1) * DH)
                        last = nc.tensor.matmul(o_ps[rows, q], v_ring[:, v_at[0], v_at[1], rows], p_view[:, p_slot, head, q],
                                                start=start, stop=stop)
                last.then_inc(pv_done, 1)

            pe.wait_ge(consts_ready, 2)
            pe.wait_ge(zeros_ready, 1)
            for _ in range(WARM_UP):
                nc.tensor.matmul(v_ps[0:DH, :], ones[:, :], o_raw[:, 0:QH], start=True, stop=True)

            pe.wait_ge(w_loaded[0], 16)
            pe.wait_ge(ctx_loaded[0], 16)
            project_k(0, 0, None)
            pe.wait_ge(wq0_loaded, 32)
            pe.wait_ge(x_loaded, 16)
            for n in range(4):
                project_q(q0_ps[n], n, 0)
            pe.wait_ge(wv0_loaded, 16)
            project_v(v_place(0)[1], 0, 0).then_inc(v_proj_done, 1)
            pe.wait_ge(kq_split, PRO_USES)
            scores(0, 0, None)

            def pair_body(pair, parity, first, last):
                g0 = CHUNKS * pair
                if not first:
                    pe.wait_ge(den_taken, NQH * pair)

                def chunk_scores(c, k, looped):
                    if k == CHUNKS and not looped:
                        if not last:
                            pe.wait_ge(kq_split, use(pair, PAIR_USES - 1))
                            scores(0, 1 - parity, 2 * (g0 + c - 1))
                        return
                    if k % BLOCK == 0:
                        if looped:
                            pe.wait_ge(kq_split, use(pair, 0) + (c - k) // BLOCK + k // BLOCK - 1)
                        else:
                            pe.wait_ge(kq_split, use(pair, k_use(k // BLOCK, last)))
                    scores(cols_of(k, looped), parity, 2 * (g0 + c - 1))

                def projection(c, k, looped, place):
                    found = use_in(pair, c, k, looped, place, last)
                    if found is None:
                        return
                    count, what, b, s = found
                    if what == "q":
                        if b == 0:
                            pe.wait_ge(w_loaded[1 - parity], w_need(pair, parity, first))
                        pe.wait_ge(kq_split, count - 1)
                        project_q(kq_ps[:, :], b, 1 - parity)
                        return
                    turns = FULL_BLOCKS // RING
                    if looped:
                        pe.wait_ge(ctx_loaded[s], (turns * pair + (c - k) // LOOP_CHUNKS
                                                   + ((k + 1) // BLOCK + 1) // RING + 1) * 16)
                    elif s == TAIL_SLOT:
                        pe.wait_ge(ctx_loaded[s], pair * 16 + 16)
                        if first:
                            pe.wait_ge(consts_ready, 2)
                    else:
                        pe.wait_ge(ctx_loaded[s], pair * (16 * turns) + 16 * (b // RING + 1 if b else turns + 1))
                    project_k(s, 1 - parity if b == 0 else parity, count - 1)

                def step(c, k, looped):
                    todo = chunks_of(c, k)
                    chunk_scores(*todo[0], looped)
                    projection(c, k, looped, "mid")
                    pe.wait_ge(v_ready, groups(pair, -1) + (c + 1) // 2)
                    for following, n in todo:
                        if n == CHUNKS and not looped:
                            if not last:
                                group = project_v(v_place(0)[1], 0, 1 - parity)
                        else:
                            group = project_v(v_place(n)[1], cols_of(n, looped), parity)
                    group.then_inc(v_proj_done, 1)
                    if len(todo) > 1:
                        chunk_scores(*todo[1], looped)
                    if k == 0 and not looped and not first:
                        pe.wait_ge(o_raw_ready, NQH * pair)
                    if k == 0:
                        pv(0, v_place(0), True, False)
                    else:
                        pv(k % RING, v_place(k), False, False)
                        pe.wait_ge(v_ready, groups(pair, 0) + (c + 1) // 2)
                        ends = not looped and k + 2 == CHUNKS
                        if ends and last:
                            pe.wait_ge(probs_ready, 2 * (g0 + CHUNKS))
                        pv((k + 1) % RING, v_place(k + 1), False, ends)
                    projection(c, k, looped, "end")

                run_steps(pe, step)
                pe.wait_ge(sums_done, 2 * (g0 + CHUNKS) + SUM_CREDIT)
                if first:
                    pe.wait_ge(consts_ready, 2)
                for h in range(NQH):
                    if h == 0:
                        pe.wait_ge(kq_split, use(pair, LOOP_USES + len(straight_uses(last)) - 1))
                    else:
                        pe.wait_ge(v_ready, groups(pair, V_GROUPS - 1))
                    for head in range(2):
                        rows = slice(head * DH, (head + 1) * DH)
                        last_mm = nc.tensor.matmul(den_ps[h][rows, :], ones[:, :],
                                                   sums[:, parity, head, h * QH:(h + 1) * QH], start=True, stop=True)
                    last_mm.then_inc(den_done, 1)

            def w_need(pair, parity, first):
                if first:
                    return 64
                return 32 * pair + (16 + 32 if parity else 64)

            run_pairs(pe, pair_body)

            def project_output(t, pairs):
                for pair in pairs:
                    last = nc.tensor.matmul(y_ps[t], attn[:, pair, t * P:(t + 1) * P], wo_sb[:, pair, :],
                                            start=(pair == 0), stop=(pair == PAIRS - 1))
                return last

            pe.wait_ge(xres_loaded, 32)
            pe.wait_ge(norm_done, NQH * (PAIRS - 1))
            for t in range(QT // 2):
                project_output(t, range(PAIRS - 1))
            for t in range(QT):
                pe.wait_ge(norm_done, NQH * (PAIRS - 1) + 2 * t // QT + 1)
                if t >= QT // 2:
                    pe.wait_ge(o_raw_ready, NQH * PAIRS)
                    pe.wait_ge(den_taken, NQH * PAIRS)
                project_output(t, range(PAIRS) if t >= QT // 2 else [PAIRS - 1]).then_inc(y_done, 1)

            pe.wait_ge(y_taken, QT)
            pe.wait_ge(exact_ready, 1)
            nc.tensor.matmul(s_ps[0:1, 0, 0:1], exact[:, :], ones[:, 0:1], start=True, stop=True).then_inc(exact_counted, 1)

            def general():
                pe.wait_ge(identity_ready, 2)

                def queries(pair, t):
                    pe.wait_ge(g_w_loaded, 48 * pair + 48)
                    pe.wait_ge(g_taken, G_TAKES * 2 * QT * pair + G_TAKES * 2 * t + 1)
                    nc.tensor.matmul(kq_ps[:, 0:P], g_w[:, 0, :], xT_sb[:, bass.ds(t * P, P)],
                                     start=True, stop=True).then_inc(g_q_done, 1)

                def head_of_tile(pair, t, head, n):
                    rows = slice(head * DH, (head + 1) * DH)

                    def block_scores(b, slot):
                        if slot != TAIL_SLOT:
                            pe.wait_ge(g_ctx_loaded, n * (32 * FULL_BLOCKS) + b * 16 + 16)
                        pe.wait_ge(g_q_ready, QT * pair + t + 1)
                        pe.wait_ge(g_taken, G_TAKES * n + b + 1)
                        cols = TAIL_COLS if slot == TAIL_SLOT else BK
                        nc.tensor.matmul(kq_ps[:, 0:cols], g_w[:, 1, :], ctx_ring[:, slot * BK:slot * BK + cols],
                                         start=True, stop=True).then_inc(g_k_done, 1)
                        pe.wait_ge(g_k_ready, G_BLOCKS * n + b + 1)
                        nc.tensor.matmul(s_ps[:, 0, 0:cols], g_q[rows, :], g_k[rows, 0:cols],
                                         start=True, stop=True).then_inc(g_s_done, 1)

                    g_blocks(pe, block_scores)

                    def block_product(b, slot):
                        if slot != TAIL_SLOT:
                            pe.wait_ge(g_ctx_loaded, n * (32 * FULL_BLOCKS) + b * 16 + (16 * FULL_BLOCKS + 16))
                        for m in range(G_CHUNKS_TAIL if slot == TAIL_SLOT else BLOCK):
                            k = CHUNKS * n + BLOCK * b + m
                            pe.wait_ge(g_p_ready, k + 1)
                            cols = slot * BK + m * P
                            nc.tensor.matmul(v_ps[:, 0:2 * DH], ctx_ring[:, cols:cols + P], g_w[:, 2, :],
                                             start=True, stop=True)
                            nc.tensor.transpose(kq_ps[:, 0:P], g_p[:, :], identity[:, :]).then_inc(g_vp_done, 1)
                            pe.wait_ge(g_vp_ready, k + 1)
                            nc.tensor.matmul(o_ps[rows, 0:P], g_v[:, rows], g_pT[:, :],
                                             start=True, stop=True).then_inc(g_pv_done, 1)

                    g_blocks(pe, block_product)

                g_loops(pe, g_nothing, queries, head_of_tile)
                pe.wait_ge(g_attn_done, 2 * QT * PAIRS)
                for t in range(QT):
                    project_output(t, range(PAIRS)).then_inc(y_done, 1)

            if_general(pe, general)

        @block.scalar
        def _(act):
            def high_k(slot):
                n = TAIL_COLS if slot == TAIL_SLOT else BK
                cols = slice(slot * BK, slot * BK + n)
                nc.scalar.activation(k_parts[0:DH, 0, cols], kq_ps[0:DH, 0:n], ACT.Copy)
                nc.scalar.activation(k_parts[DH:P, 1, cols], kq_ps[DH:P, 0:n], ACT.Copy).then_inc(kq_high_ready, 1)

            def high_q(src, n, parity):
                head, h = n // NQH, n % NQH
                nc.scalar.activation(q_parts[:, parity, head, 0, h * QH:(h + 1) * QH], src,
                                     ACT.Copy).then_inc(kq_high_ready, 1)

            def exps(g, p_slot):
                act.wait_ge(pv_done, g + (PV_CREDIT - RING + 1))
                act.wait_ge(sums_done, 2 * g + (SUM_CREDIT - 2 * RING + 2))
                for head in range(2):
                    act.wait_ge(scores_ready, 2 * g + head + 1)
                    nc.scalar.activation(p_view[:, p_slot, head, :], s_ps[:, head, :], ACT.Exp,
                                         scale=SCALE).then_inc(probs_ready, 1)

            src_q = w_q[:, 0:2 * DH].rearrange("p (h n) -> p h n", h=2)
            for copy in range(2):
                act.dma_start(wq_dup[:, 0, :, copy, :], src_q).then_inc(wq0_loaded, 16)
            act.dma_start(xT_sb[:, :], xT).then_inc(x_loaded, 16)
            act.wait_ge(kq_proj_done, 1)
            high_k(0)
            for n in range(4):
                act.wait_ge(kq_proj_done, n + 2)
                high_q(q0_ps[n], n, 0)
            exps(0, 0)

            def pair_body(pair, parity, first, last):
                g0 = CHUNKS * pair

                def high_halves(c, k, looped, place):
                    found = use_in(pair, c, k, looped, place, last)
                    if found is not None:
                        count, what, b, s = found
                        act.wait_ge(kq_proj_done, count)
                        if what == "q":
                            high_q(kq_ps[:, :], b, 1 - parity)
                        else:
                            high_k(s)

                def step(c, k, looped):
                    for n, (chunk, m) in enumerate(chunks_of(c, k)):
                        if not (last and not looped and m == CHUNKS):
                            exps(g0 + chunk, m % RING)
                        if n == 0:
                            high_halves(c, k, looped, "mid")
                    high_halves(c, k, looped, "end")

                run_steps(act, step)
                act.wait_ge(pv_done, g0 + CHUNKS + PV_CREDIT)
                for h in range(NQH):
                    if not first:
                        act.wait_ge(norm_done, NQH * (pair - 1) + h + 1)
                    nc.scalar.activation(o_raw[:, h * QH:(h + 1) * QH], o_ps[:, h * QH:(h + 1) * QH],
                                         ACT.Copy).then_inc(o_raw_ready, 1)

            run_pairs(act, pair_body)
            def general():
                def head_of_tile(pair, t, head, n):
                    def copy_k(b, slot):
                        cols = TAIL_COLS if slot == TAIL_SLOT else BK
                        act.wait_ge(g_k_done, G_BLOCKS * n + b + 1)
                        nc.scalar.activation(g_k[:, 0:cols], kq_ps[:, 0:cols], ACT.Copy).then_inc(g_k_ready, 1)

                    g_blocks(act, copy_k)
                    act.wait_ge(g_row_step, 5 * n + 2)
                    nc.scalar.activation(g_row[:, 0:NK], g_row[:, 0:NK], ACT.Exp, bias=g_bias[:, 0:1], scale=SCALE,
                                         accum_out=g_sum[:, 0:1]).then_inc(g_exp_done, 1)

                    def copy_vp(b, slot):
                        for m in range(G_CHUNKS_TAIL if slot == TAIL_SLOT else BLOCK):
                            act.wait_ge(g_vp_done, CHUNKS * n + BLOCK * b + m + 1)
                            nc.scalar.activation(g_v[:, :], v_ps[:, 0:2 * DH], ACT.Copy)
                            nc.scalar.activation(g_pT[:, :], kq_ps[:, 0:P], ACT.Copy).then_inc(g_vp_ready, 1)

                    g_blocks(act, copy_vp)

                g_loops(act, g_nothing, g_nothing, head_of_tile)

            def roots(turn):
                for n in range(QT // 2):
                    act.wait_ge(inv_var_ready, QT // 2 * turn + n + 1)
                    ts = slice(2 * n, 2 * n + 2)
                    nc.scalar.activation(rstd[:, ts], inv_var[:, ts], ACT.Sqrt).then_inc(rstd_ready, 1)

            def general_and_roots():
                general()
                roots(1)

            act.wait_ge(consts_ready, 2)
            nc.scalar.activation(rstd[:, 0:1], ones[:, 0:1], ACT.Sqrt).then_inc(table_loaded, 1)
            act.wait_ge(table_loaded, 1)
            roots(0)
            if_general(act, general_and_roots)

        @block.vector
        def _(dve):
            dve.sem_inc(sums_done, SUM_CREDIT)
            nc.vector.memset(o_raw[:, 0:QH], 0.0).then_inc(zeros_ready, 1)

            def low_k(slot):
                n = TAIL_COLS if slot == TAIL_SLOT else BK
                cols = slice(slot * BK, slot * BK + n)
                nc.vector.tensor_tensor(out=k_parts[DH:P, 0, cols], in0=kq_ps[0:DH, 0:n],
                                        in1=k_parts[0:DH, 0, cols].bitcast(F32), op=ALU.subtract)
                nc.vector.tensor_tensor(out=k_parts[0:DH, 1, cols], in0=kq_ps[DH:P, 0:n],
                                        in1=k_parts[DH:P, 1, cols].bitcast(F32), op=ALU.subtract).then_inc(kq_split, 1)

            def low_q(src, n, parity):
                head, h = n // NQH, n % NQH
                q = slice(h * QH, (h + 1) * QH)
                nc.vector.tensor_tensor(out=q_parts[:, parity, head, 1, q], in0=src,
                                        in1=q_parts[:, parity, head, 0, q].bitcast(F32),
                                        op=ALU.subtract).then_inc(kq_split, 1)

            def take_v(count, place, n, pv_before):
                dve.wait_ge(v_proj_done, count)
                dve.wait_ge(pv_done, pv_before + PV_CREDIT)
                group, pos = place
                nc.vector.tensor_copy(v_ring[:, group, pos:pos + n, :].rearrange("p n d -> p (n d)"),
                                      v_ps[:, pos * P:(pos + n) * P]).then_inc(v_ready, 1)

            def add_sums(g, p_slot, parity, new, rows):
                for head in range(2):
                    dve.wait_ge(probs_ready, 2 * g + head + 1)
                    if new:
                        nc.vector.tensor_copy(sums[:, parity, head, :], p_view[:, p_slot, head, :]).then_inc(sums_done, 1)
                    else:
                        dve.wait_ge(sums_done, 2 * g + head + (SUM_CREDIT - 1))
                        nc.vector.tensor_tensor(out=sums[0:rows, parity, head, :], in0=sums[0:rows, parity, head, :],
                                                in1=p_view[0:rows, p_slot, head, :], op=ALU.add).then_inc(sums_done, 1)

            def invert_sums(pair, n):
                w = NQ // INV_PIECES
                dve.wait_ge(den_taken, NQH * pair + n * NQH // INV_PIECES + 1)
                nc.vector.reciprocal(inv_sum[:, n * w:(n + 1) * w], inv_sum[:, n * w:(n + 1) * w]).then_inc(inv_ready, 1)

            def find_limit(pair, n):
                dve.wait_ge(inv_ready, INV_PIECES * pair + INV_PIECES)
                nc.vector.tensor_reduce(out=limits[:, n, bass.ds(pair, 1)], in_=inv_sum[:, :], axis=AX.X,
                                        op=(ALU.add, ALU.min)[n]).then_inc(limits_done, 1)

            dve.wait_ge(kq_high_ready, 1)
            low_k(0)
            for n in range(4):
                dve.wait_ge(kq_high_ready, n + 2)
                low_q(q0_ps[n], n, 0)
            take_v(1, v_place(0), 1, 0)
            add_sums(0, 0, 0, True, P)

            def pair_body(pair, parity, first, last):
                g0 = CHUNKS * pair

                def low_halves(c, k, looped, place):
                    found = use_in(pair, c, k, looped, place, last)
                    if found is not None:
                        count, what, b, s = found
                        dve.wait_ge(kq_high_ready, count)
                        if what == "q":
                            low_q(kq_ps[:, :], b, 1 - parity)
                        else:
                            low_k(s)

                def step(c, k, looped):
                    todo = chunks_of(c, k)
                    if k == 0:
                        take_v(groups(pair, 0), v_place(1), 1, g0)
                    else:
                        alone = last and not looped and k + 2 == CHUNKS
                        take_v(groups(pair, 0) + (c + 1) // 2, v_place(k + 1), 1 if alone else 2, g0 + c)
                    for n, (chunk, m) in enumerate(todo):
                        if not looped and m == CHUNKS:
                            if not last:
                                add_sums(g0 + chunk, 0, 1 - parity, True, P)
                        else:
                            add_sums(g0 + chunk, m % RING, parity, False,
                                     LAST_KEYS if not looped and m + 1 == CHUNKS else P)
                        if n == 0:
                            low_halves(c, k, looped, "mid")
                    low_halves(c, k, looped, "end")
                    if not first and not looped and c in INV_STEPS:
                        invert_sums(pair - 1, INV_STEPS.index(c))
                    if not first and not looped and c in LIMIT_STEPS:
                        find_limit(pair - 1, LIMIT_STEPS.index(c))

                run_steps(dve, step)
                for h in range(NQH):
                    dve.wait_ge(den_done, NQH * pair + h + 1)
                    if not first:
                        dve.wait_ge(norm_done, NQH * (pair - 1) + h + 1)
                        dve.wait_ge(limits_done, 2 * pair)
                    nc.vector.tensor_copy(inv_sum[:, h * QH:(h + 1) * QH], den_ps[h][:, :]).then_inc(den_taken, 1)
                if last:
                    for n in range(INV_PIECES):
                        invert_sums(pair, n)

            run_pairs(dve, pair_body)

            def layer_norm(turn):
                STEPS = 5
                for n in range(QT // 2):
                    before = STEPS * (QT // 2 * turn + n)
                    tiles = (2 * n, 2 * n + 1)
                    for t in tiles:
                        dve.wait_ge(y_done, QT * turn + t + 1)
                        nc.vector.tensor_tensor(out=y[:, t, :], in0=y_ps[t], in1=x_sb[:, t, :],
                                                op=ALU.add).then_inc(y_taken, 1)
                    for t in tiles:
                        dve.wait_ge(y_taken, QT * turn + t + 1)
                        nc.vector.bn_stats(stats[:, t, :], y[:, t, :]).then_inc(ln_step, 1)
                    for m, t in enumerate(tiles):
                        dve.wait_ge(ln_step, before + m + 1)
                        nc.vector.bn_aggr(mean_var[:, t, :], stats[:, t, :]).then_inc(ln_step, 1)
                    dve.wait_ge(ln_step, before + 4)
                    ts = slice(2 * n, 2 * n + 2)
                    nc.vector.tensor_scalar(out=inv_var[:, ts], in0=mean_var[:, ts, 1], scalar1=EPS, scalar2=None,
                                            op0=ALU.add).then_inc(ln_step, 1)
                    dve.wait_ge(ln_step, before + 5)
                    nc.vector.reciprocal(inv_var[:, ts], inv_var[:, ts]).then_inc(inv_var_ready, 1)
                    dve.wait_ge(rstd_ready, QT // 2 * turn + n + 1)
                    for t in tiles:
                        nc.vector.tensor_scalar(out=y[:, t, :], in0=y[:, t, :], scalar1=mean_var[:, t, 0:1],
                                                scalar2=rstd[:, t:t + 1], op0=ALU.subtract,
                                                op1=ALU.mult).then_inc(ln_done, 1)

            dve.wait_ge(xres_loaded, 32)
            layer_norm(0)

            for n in range(2):
                find_limit(PAIRS - 1, n)
            dve.wait_ge(limits_done, 2 * PAIRS)
            for n, extreme in enumerate((ALU.add, ALU.min)):
                nc.vector.tensor_reduce(out=extremes[:, n:n + 1], in_=limits[:, n, :], axis=AX.X,
                                        op=extreme).then_inc(range_step, 1)
            dve.wait_ge(range_step, 2)
            for n, (bound, within) in enumerate(((1 / SUM_LEAST, ALU.is_lt), (1 / SUM_MOST, ALU.is_ge))):
                nc.vector.tensor_scalar(out=in_range[:, n:n + 1], in0=extremes[:, n:n + 1], scalar1=bound, scalar2=None,
                                        op0=within).then_inc(range_step, 1)
            dve.wait_ge(range_step, 4)
            nc.vector.tensor_tensor(out=exact[:, :], in0=in_range[:, 0:1], in1=in_range[:, 1:2],
                                    op=ALU.mult).then_inc(exact_ready, 1)
            dve.wait_ge(exact_counted, 1)
            nc.vector.tensor_scalar(out=use_general[:, :], in0=s_ps[0:1, 0, 0:1], scalar1=P - 0.5, scalar2=None,
                                    op0=ALU.is_lt).then_inc(choice_ready, 1)

            def general():
                dve.wait_ge(norm_done, NQH * PAIRS)
                dve.sem_inc(g_taken, 1)
                nc.vector.memset(g_row[:, NK:CHUNKS * P], 0.0)

                def queries(pair, t):
                    dve.wait_ge(g_q_done, QT * pair + t + 1)
                    nc.vector.tensor_copy(g_q[:, :], kq_ps[:, 0:P]).then_inc(g_q_ready, 1)

                def head_of_tile(pair, t, head, n):
                    rows = slice(head * DH, (head + 1) * DH)

                    def take_scores(b, slot):
                        cols = TAIL_KEYS if slot == TAIL_SLOT else BK
                        dve.wait_ge(g_s_done, G_BLOCKS * n + b + 1)
                        nc.vector.tensor_copy(g_row[:, bass.ds(b * BK, cols)], s_ps[:, 0, 0:cols]).then_inc(g_taken, 1)

                    g_blocks(dve, take_scores)
                    dve.wait_ge(g_taken, G_TAKES * n + (G_BLOCKS + 1))
                    nc.vector.tensor_reduce(out=g_max[:, :], in_=g_row[:, 0:NK], axis=AX.X,
                                            op=ALU.max).then_inc(g_row_step, 1)
                    dve.wait_ge(g_row_step, 5 * n + 1)
                    nc.vector.tensor_scalar(out=g_bias[:, :], in0=g_max[:, :], scalar1=-SCALE, scalar2=None,
                                            op0=ALU.mult).then_inc(g_row_step, 1)
                    dve.wait_ge(g_exp_done, n + 1)
                    nc.vector.reciprocal(g_inv[:, :], g_sum[:, :]).then_inc(g_row_step, 1)
                    dve.wait_ge(g_row_step, 5 * n + 3)
                    nc.vector.tensor_scalar(out=g_row[:, 0:NK], in0=g_row[:, 0:NK], scalar1=g_inv[:, 0:1], scalar2=None,
                                            op0=ALU.mult).then_inc(g_row_step, 1)
                    dve.wait_ge(g_row_step, 5 * n + 4)
                    nc.vector.memset(g_acc[rows, :], 0.0).then_inc(g_row_step, 1)

                    def take_products(b, slot):
                        for m in range(G_CHUNKS_TAIL if slot == TAIL_SLOT else BLOCK):
                            nc.vector.tensor_copy(g_p[:, :], g_row[:, bass.ds(b * BK + m * P, P)]).then_inc(g_p_ready, 1)
                            dve.wait_ge(g_row_step, 5 * n + 5)
                            dve.wait_ge(g_pv_done, CHUNKS * n + BLOCK * b + m + 1)
                            dve.wait_ge(g_taken, G_TAKES * n + BLOCK * b + (G_BLOCKS + m + 1))
                            nc.vector.tensor_tensor(out=g_acc[rows, :], in0=g_acc[rows, :], in1=o_ps[rows, 0:P],
                                                    op=ALU.add).then_inc(g_taken, 1)

                    g_blocks(dve, take_products)
                    dve.wait_ge(g_taken, G_TAKES * n + (G_TAKES + 1))
                    nc.vector.tensor_copy(attn[rows, bass.ds(pair, 1), bass.ds(t * P, P)].rearrange("p a q -> p (a q)"),
                                          g_acc[rows, :]).then_inc(g_attn_done, 1)

                g_loops(dve, g_nothing, queries, head_of_tile)

            def general_and_norm():
                general()
                dve.wait_ge(stored, 16 * (QT // 2))
                layer_norm(1)

            if_general(dve, general_and_norm)


def kernel(**inputs):
    import numpy as np
    import concourse.bacc as bacc
    from concourse import mybir as mb
    from concourse.bass_utils import run_bass_kernel_spmd

    x = np.asarray(inputs["x"])[0]
    context = np.asarray(inputs["ctx_1024"])[0]
    arrays = {
        "in_xT": np.ascontiguousarray(x.T),
        "in_x": np.ascontiguousarray(x),
        "in_ctxT": np.ascontiguousarray(context.T),
        "in_wq": np.ascontiguousarray(inputs["L0_xattn_W_Q"]),
        "in_wk": np.ascontiguousarray(inputs["L0_xattn_W_K"]),
        "in_wv": np.ascontiguousarray(inputs["L0_xattn_W_V"]),
        "in_wo": np.ascontiguousarray(inputs["L0_xattn_W_O"]),
    }
    nc = bacc.Bacc("TRN2", target_bir_lowering=False, num_devices=1)
    args = [nc.dram_tensor(n, a.shape, mb.dt.from_np(a.dtype), kind="ExternalInput").ap() for n, a in arrays.items()]
    out = nc.dram_tensor("out_0", x.shape, mb.dt.from_np(x.dtype), kind="ExternalOutput").ap()
    cross_attention_kernel(nc, *args, out)
    r = run_bass_kernel_spmd(nc, [arrays], core_ids=[0])
    return r.results[0]["out_0"].reshape(1, *x.shape)
```
